# Optimizing a Trainium2 kernel written in Bass

```python
import numpy as np
import jax
import jax.numpy as jnp

def _softmax(x, axis=-1):
    return jax.nn.softmax(x, axis=axis)

def _gelu(x):
    return jax.nn.gelu(x, approximate=True)

def _silu(x):
    return jax.nn.silu(x)

def _sigmoid(x):
    return jax.nn.sigmoid(x)

def _layernorm(x, axis=-1, eps=1e-05):
    m = jnp.mean(x, axis=axis, keepdims=True)
    v = jnp.var(x, axis=axis, keepdims=True)
    return (x - m) / jnp.sqrt(v + eps)

def _scatter_add(tgt, idx, src, axis=0):
    return tgt.at[idx].add(src)

def _segment_sum(src, seg, n):
    return jax.ops.segment_sum(src, seg, n)
kernel_name = 'mk_rec_standalone_d1_rec_r8_55eb64'

def setup_inputs(seed: int=0):
    np.random.seed(seed)
    _w = jnp.asarray

    def _rec_inputs():
        import jax
        import jax.numpy as jnp
        _rk = jax.random.key(seed)
        r_x = -0.000849101 + 1.0004 * jax.random.normal(jax.random.fold_in(_rk, 1), (512, 39, 16), jnp.float32)
        return r_x
    r_x = _rec_inputs()

    def _L0_rec_setup():
        import jax, jax.numpy as jnp
        import numpy as np
        LAYER_SIZES = [128, 128, 128]
        F0 = 39
        D = 16
        B = 256
        key = jax.random.key(seed)
        ks = jax.random.split(key, 4)
        field_nums = [F0, LAYER_SIZES[0] // 2, LAYER_SIZES[1] // 2]
        x = jax.random.normal(ks[0], (B, F0, D), dtype=jnp.float32)
        W0 = jax.random.normal(ks[1], (F0 * field_nums[0], LAYER_SIZES[0]), dtype=jnp.float32) * 0.05
        W1 = jax.random.normal(ks[2], (F0 * field_nums[1], LAYER_SIZES[1]), dtype=jnp.float32) * 0.05
        W2 = jax.random.normal(ks[3], (F0 * field_nums[2], LAYER_SIZES[2]), dtype=jnp.float32) * 0.05
        b0 = jnp.zeros((LAYER_SIZES[0],), jnp.float32)
        b1 = jnp.zeros((LAYER_SIZES[1],), jnp.float32)
        b2 = jnp.zeros((LAYER_SIZES[2],), jnp.float32)
        return {'x': x, 'W0': W0, 'W1': W1, 'W2': W2, 'b0': b0, 'b1': b1, 'b2': b2}
    _L0_rec_all = _L0_rec_setup()
    _L0_rec_in = {k: v for k, v in _L0_rec_all.items() if k in ('W0', 'W1', 'W2', 'b0', 'b1', 'b2')}
    del _L0_rec_all
    return {'r_x': r_x, 'L0_rec_W0': _L0_rec_in['W0'], 'L0_rec_W1': _L0_rec_in['W1'], 'L0_rec_W2': _L0_rec_in['W2'], 'L0_rec_b0': _L0_rec_in['b0'], 'L0_rec_b1': _L0_rec_in['b1'], 'L0_rec_b2': _L0_rec_in['b2']}

def reference(r_x, L0_rec_W0, L0_rec_W1, L0_rec_W2, L0_rec_b0, L0_rec_b1, L0_rec_b2):
    import jax
    import jax.numpy as jnp

    def _L0_rec_ref(x, W0, W1, W2, b0, b1, b2):
        import jax, jax.numpy as jnp
        import numpy as np
        LAYER_SIZES = [128, 128, 128]
        F0 = 39
        D = 16
        B = 256
        Ws = [W0, W1, W2]
        bs = [b0, b1, b2]
        h = x
        outs = []
        n_layers = len(LAYER_SIZES)
        for i, S in enumerate(LAYER_SIZES):
            Fk = h.shape[1]
            Wr = Ws[i].reshape(F0, Fk, S)
            out = jax.nn.relu(jnp.einsum('bfd,bgd,fgs->bsd', x, h, Wr) + bs[i][None, :, None])
            if i != n_layers - 1:
                h, direct = (out[:, :S // 2], out[:, S // 2:])
            else:
                direct = out
            outs.append(direct)
        result = jnp.concatenate(outs, axis=1)
        return jnp.sum(result, axis=-1)
    y = _L0_rec_ref(r_x, L0_rec_W0, L0_rec_W1, L0_rec_W2, L0_rec_b0, L0_rec_b1, L0_rec_b2)
    return y

_drawn_inputs = setup_inputs


def setup_inputs(seed=0):
    import zlib

    import numpy as np

    out = dict(_drawn_inputs(seed))
    spreads = {'L0_rec_b0': (0.0, 0.308), 'L0_rec_b1': (0.0, 0.481), 'L0_rec_b2': (0.0, 0.486)}
    factors = {}
    for name, (base, spread) in spreads.items():
        noise = np.random.default_rng([zlib.crc32(name.encode()), seed]).standard_normal(out[name].shape)
        drawn = base * np.exp(spread * noise) if base else spread * noise
        out[name] = jnp.asarray(drawn.astype(out[name].dtype))
    for name, factor in factors.items():
        out[name] = (out[name] * factor).astype(out[name].dtype)
    return out
```

```python
from contextlib import ExitStack

import concourse.bass as bass
from concourse import mybir

F32 = mybir.dt.float32
ALU = mybir.AluOpType
ACT = mybir.ActivationFunctionType
AX_X = mybir.AxisListType.X

FIELDS = 39
DIM = 16
BATCH = 512
SIZE = 128
HALF = SIZE // 2
COLS = BATCH * DIM
N = 512
BLOCKS = COLS // N
BB = N // DIM
PAIRS = BLOCKS // 2

SHIFTS = FIELDS // 2 + 1
PER = 3
T0 = -(-SHIFTS // PER)
P0 = PER * FIELDS
P0_LAST = (SHIFTS - PER * (T0 - 1)) * FIELDS
T12 = -(-FIELDS // 2)
G = 4
G12 = T12 // G
G0 = -(-T0 // G)
GROUPS = 2 * G12 + G0
RING = 6
AHEAD = 2


def cin(nc, x2, w0a, w0b, w1, w2, b, out):
    with ExitStack() as ctx:
        def sb(name, shape):
            return ctx.enter_context(nc.sbuf_tensor(name, shape, F32))

        def sem(name):
            return ctx.enter_context(nc.semaphore(name))

        w0 = sb("w0", [P0, T0, SIZE])
        w0t = sb("w0t", [P0, T0, SIZE])
        wsb = [None, sb("w1s", [128, T12, SIZE]), sb("w2s", [128, T12, SIZE])]
        bias = sb("bias", [128, 3])
        xrep = sb("xrep", [P0, AHEAD, N])
        xshift = sb("xshift", [P0, AHEAD, T0, N])
        xwide = sb("xwide", [128, AHEAD, T12, N])
        z = sb("z", [128, RING, G, N])
        h = [sb("h0", [128, N]), sb("h1", [128, N])]
        direct = sb("direct", [128, AHEAD, N])
        last = sb("last", [128, N])
        sums01 = sb("sums01", [128, BATCH])
        sums2 = sb("sums2", [128, BATCH])
        acc = [ctx.enter_context(nc.psum_tensor(f"acc{l}", [128, N], F32)) for l in range(3)]

        w0_in = sem("w0_in")
        w0_folded = sem("w0_folded")
        w_in = [None, sem("w1_in"), sem("w2_in")]
        bias_in = sem("bias_in")
        xs_in = [sem(f"xs_in{b}") for b in range(AHEAD)]
        xw_in = [[sem(f"xw_in{b}_{g}") for g in range(G12)] for b in range(AHEAD)]
        z_made = sem("z_made")
        z_used = sem("z_used")
        h_ready = [sem("h0_ready"), sem("h1_ready")]
        acc_read = [sem(f"acc{l}_read") for l in range(3)]
        summed = sem("summed")
        out_sent = sem("out_sent")

        direct1_ready = acc_read[1]
        last_ready = acc_read[2]

        def first_group(layer, j):
            if isinstance(j, int) and (layer, j) == (0, 0):
                return 0
            if isinstance(j, int) and (layer, j) == (2, BLOCKS - 1):
                return GROUPS * j + G0 + G12
            return {1: GROUPS * j + G0, 0: GROUPS * (j - 1) + G0 + G12, 2: GROUPS * j + G0 + G12 + G0}[layer]

        def slot_base(layer, j, par):
            return first_group(layer, j if isinstance(j, int) else par)

        block = ctx.enter_context(nc.Block())

        @block.sync
        def _(sp):
            def load_shifted(pair, par):
                for a in range(PER):
                    rows = slice(a * FIELDS, (a + 1) * FIELDS)
                    src = x2[0:FIELDS, bass.ds(N * (2 * pair + par), N)]
                    sp.dma_start(xrep[rows, par, :], src).then_inc(xs_in[par], 16)
                    src = bass.AP(x2.tensor, x2.offset + COLS * a + N * (2 * pair + par),
                                  [[COLS, FIELDS], [PER * COLS, T0], [1, N]])
                    sp.dma_start(xshift[rows, par, :, :], src).then_inc(xs_in[par], 16)

            def load_wide(pair, par, g):
                for e in range(2):
                    src = bass.AP(x2.tensor, x2.offset + COLS * (2 * G * g + e) + N * (2 * pair + par),
                                  [[0, HALF], [2 * COLS, G], [1, N]])
                    sp.dma_start(xwide[HALF * e:HALF * (e + 1), par, G * g:G * (g + 1), :],
                                 src).then_inc(xw_in[par][g], 16)

            def refill(pair, par, shifted=True):
                if shifted:
                    sp.wait_ge(z_made, first_group(2, 2 * pair + par))
                    load_shifted(pair + 1 + par, 1 - par)
                for g in range(G12):
                    sp.wait_ge(z_made, first_group(2, 2 * pair + par) + g + 1)
                    load_wide(pair + 1, par, g)

            sp.dma_start(w0[:], w0a).then_inc(w0_in, 16)
            sp.dma_start(w0t[:], w0b).then_inc(w0_in, 16)
            load_shifted(0, 0)
            sp.dma_start(bias[:], b).then_inc(bias_in, 16)
            sp.dma_start(wsb[1][:], w1).then_inc(w_in[1], 16)
            for g in range(G12):
                load_wide(0, 0, g)
            load_shifted(0, 1)
            sp.dma_start(wsb[2][:], w2).then_inc(w_in[2], 16)
            for g in range(G12):
                load_wide(0, 1, g)
            sp.wait_ge(z_made, G0)
            load_shifted(1, 0)
            with sp.Fori(0, PAIRS - 2) as pair:
                for par in range(2):
                    refill(pair, par)
            refill(PAIRS - 2, 0)
            refill(PAIRS - 2, 1, shifted=False)
            sp.wait_ge(summed, 2 * BLOCKS)
            sp.dma_start(out[0:HALF, :], sums01[HALF:SIZE, :]).then_inc(out_sent, 16)
            sp.dma_start(out[HALF:SIZE, :], sums01[0:HALF, :]).then_inc(out_sent, 16)
            sp.dma_start(out[SIZE:2 * SIZE, :], sums2[:, :]).then_inc(out_sent, 16)
            sp.wait_ge(out_sent, 48)

        @block.vector
        def _(dve):
            def make(q, slot, parts, in0, in1, tiles):
                if not isinstance(q, int) or q >= RING:
                    dve.wait_ge(z_used, q - RING + 1)
                nc.vector.tensor_tensor(z[0:parts, slot, 0:tiles, :], in0, in1,
                                        ALU.mult).then_inc(z_made, 1)

            def layer0(pair, par, q0, slot0):
                dve.wait_ge(xs_in[par], 32 * PER * (pair + 1))
                for g in range(G0):
                    n = min(G, T0 - G * g)
                    make(q0 + g, (slot0 + g) % RING, P0,
                         xrep[:, par:par + 1, :].to_broadcast([P0, n, N]),
                         xshift[:, par, G * g:G * g + n, :], n)

            def layer12(layer, pair, par, after_first):
                q0 = first_group(layer, 2 * pair + par)
                slot0 = slot_base(layer, 2 * pair + par, par)
                dve.wait_ge(h_ready[layer - 1], 2 * (2 * pair + par + 1))
                for g in range(G12):
                    if layer == 1:
                        dve.wait_ge(xw_in[par][g], 32 * (pair + 1))
                    make(q0 + g, (slot0 + g) % RING, 128,
                         h[layer - 1][:, None, :].to_broadcast([128, G, N]),
                         xwide[:, par, G * g:G * (g + 1), :], G)
                    if g == 0:
                        after_first()

            def sum01(pair, par):
                dve.wait_ge(direct1_ready, 2 * pair + par + 1)
                nc.vector.tensor_reduce(sums01[:, bass.ds(BB * (2 * pair + par), BB)],
                                        direct[:, par, :].rearrange("p (b d) -> p b d", d=DIM),
                                        AX_X, ALU.add).then_inc(summed, 1)

            def sum2(pair, par):
                dve.wait_ge(last_ready, 2 * pair + par + 1)
                nc.vector.tensor_reduce(sums2[:, bass.ds(BB * (2 * pair + par), BB)],
                                        last[:].rearrange("p (b d) -> p b d", d=DIM),
                                        AX_X, ALU.add).then_inc(summed, 1)

            def one(pair, par, more=True, sum_before=True):
                layer12(1, pair, par, lambda: None)
                if more:
                    layer0(pair + par, 1 - par, first_group(0, 2 * pair + par + 1), first_group(0, par + 1))

                def sums():
                    sum01(pair, par)
                    if sum_before:
                        sum2(pair + par - 1, 1 - par)
                layer12(2, pair, par, sums)

            dve.wait_ge(w0_in, 32)
            nc.vector.tensor_tensor(w0[:], w0[:], w0t[:], ALU.add).then_inc(w0_folded, 1)
            layer0(0, 0, 0, 0)
            one(0, 0, sum_before=False)
            one(0, 1)
            with dve.Fori(1, PAIRS - 1) as pair:
                for par in range(2):
                    one(pair, par)
            one(PAIRS - 1, 0)
            one(PAIRS - 1, 1, more=False)
            sum2(PAIRS - 1, 1)

        @block.tensor
        def _(pe):
            def contract(layer, q0, slot0, read_before):
                tiles = T0 if layer == 0 else T12
                w = w0 if layer == 0 else wsb[layer]
                if not isinstance(read_before, int) or read_before > 0:
                    pe.wait_ge(acc_read[layer], read_before)
                for t in range(tiles):
                    g = t // G
                    if t % G == 0:
                        pe.wait_ge(z_made, q0 + g + 1)
                    if layer == 0:
                        rows = P0 if t < T0 - 1 else P0_LAST
                    else:
                        rows = 128 if t < T12 - 1 else HALF
                    mm = nc.tensor.matmul(acc[layer][:, :], w[0:rows, t, :],
                                          z[0:rows, (slot0 + g) % RING, t % G, :],
                                          start=(t == 0), stop=(t == tiles - 1))
                    if t % G == G - 1 or t == tiles - 1:
                        mm.then_inc(z_used, 1)

            def one(pair, par, more=True):
                j = 2 * pair + par
                contract(1, first_group(1, j), slot_base(1, j, par), j)
                if more:
                    contract(0, first_group(0, j + 1), first_group(0, par + 1), j + 1)
                contract(2, first_group(2, j), slot_base(2, j, par), j)

            pe.wait_ge(w0_folded, 1)
            contract(0, 0, 0, 0)
            pe.wait_ge(w_in[1], 16)
            pe.wait_ge(w_in[2], 16)
            one(0, 0)
            one(0, 1)
            with pe.Fori(1, PAIRS - 1) as pair:
                for par in range(2):
                    one(pair, par)
            one(PAIRS - 1, 0)
            one(PAIRS - 1, 1, more=False)

        @block.scalar
        def _(act):
            RELU = ACT.Relu

            def relu(dst, src, layer, rows):
                return nc.scalar.activation(dst, src, RELU, bias=bias[rows, layer:layer + 1])

            def wait_acc(layer, j):
                act.wait_ge(z_used, first_group(layer, j) + (G12 if layer else G0))

            def layer0(pair, par):
                wait_acc(0, 2 * pair + par)
                relu(h[0][0:HALF, :], acc[0][0:HALF, :], 0, slice(0, HALF)).then_inc(h_ready[0], 1)
                relu(h[0][HALF:, :], acc[0][0:HALF, :], 0, slice(0, HALF)).then_inc(h_ready[0], 1)
                relu(direct[HALF:, par, :], acc[0][HALF:, :], 0, slice(HALF, SIZE)).then_inc(acc_read[0], 1)

            def one(pair, par, more=True):
                wait_acc(1, 2 * pair + par)
                relu(h[1][0:HALF, :], acc[1][HALF:, :], 1, slice(HALF, SIZE)).then_inc(h_ready[1], 1)
                relu(h[1][HALF:, :], acc[1][HALF:, :], 1, slice(HALF, SIZE)).then_inc(h_ready[1], 1)
                relu(direct[0:HALF, par, :], acc[1][0:HALF, :], 1, slice(0, HALF)).then_inc(acc_read[1], 1)
                if more:
                    layer0(pair + par, 1 - par)
                wait_acc(2, 2 * pair + par)
                relu(last[:], acc[2][:, :], 2, slice(0, SIZE)).then_inc(acc_read[2], 1)

            act.wait_ge(bias_in, 16)
            layer0(0, 0)
            with act.Fori(0, PAIRS - 1) as pair:
                for par in range(2):
                    one(pair, par)
            one(PAIRS - 1, 0)
            one(PAIRS - 1, 1, more=False)


def kernel(r_x, L0_rec_W0, L0_rec_W1, L0_rec_W2, L0_rec_b0, L0_rec_b1, L0_rec_b2):
    import numpy as np
    import concourse.bacc as bacc
    from concourse.bass_utils import run_bass_kernel_spmd

    x = np.asarray(r_x).transpose(1, 0, 2).reshape(FIELDS, COLS)
    w0 = np.asarray(L0_rec_W0).reshape(FIELDS, FIELDS, SIZE)
    w0a = np.zeros((PER, FIELDS, T0, SIZE), np.float32)
    w0b = np.zeros((PER, FIELDS, T0, SIZE), np.float32)
    f = np.arange(FIELDS)
    for s in range(SHIFTS):
        g = (f + s) % FIELDS
        w0a[s % PER, :, s // PER] = w0[f, g]
        if s:
            w0b[s % PER, :, s // PER] = w0[g, f]

    def tiled(w):
        rows = np.zeros((T12 * 128, SIZE), np.float32)
        rows[:w.shape[0]] = w
        return rows.reshape(T12, 128, SIZE).transpose(1, 0, 2)

    def swapped(w):
        return np.concatenate([w[..., HALF:], w[..., :HALF]], axis=-1)

    arrays = {
        "x2": np.concatenate([x, x]),
        "w0a": w0a.reshape(P0, T0, SIZE),
        "w0b": w0b.reshape(P0, T0, SIZE),
        "w1": tiled(swapped(np.asarray(L0_rec_W1))),
        "w2": tiled(np.asarray(L0_rec_W2)),
        "b": np.stack([np.asarray(L0_rec_b0), swapped(np.asarray(L0_rec_b1)), np.asarray(L0_rec_b2)], axis=1),
    }
    arrays = {k: np.ascontiguousarray(v) for k, v in arrays.items()}
    nc = bacc.Bacc("TRN2", target_bir_lowering=False, num_devices=1)
    args = [nc.dram_tensor(k, v.shape, F32, kind="ExternalInput").ap() for k, v in arrays.items()]
    out = nc.dram_tensor("out", (2 * SIZE, BATCH), F32, kind="ExternalOutput").ap()
    cin(nc, *args, out)
    r = run_bass_kernel_spmd(nc, [arrays], core_ids=[0])
    return np.ascontiguousarray(r.results[0]["out"].T)
```

```python
from contextlib import ExitStack

import concourse.bass as bass
from concourse import mybir

F32 = mybir.dt.float32
F32R = mybir.dt.float32r
ALU = mybir.AluOpType
ACT = mybir.ActivationFunctionType
AX_X = mybir.AxisListType.X

FIELDS = 39
DIM = 16
BATCH = 512
SIZE = 128
HALF = SIZE // 2
COLS = BATCH * DIM
N = 512
BLOCKS = COLS // N
PAIRS = BLOCKS // 2
BB = N // DIM

SHIFTS = FIELDS // 2 + 1
PER = 3
T0 = -(-SHIFTS // PER)
P0 = PER * FIELDS
P0_LAST = (SHIFTS - PER * (T0 - 1)) * FIELDS
T12 = -(-FIELDS // 2)
G = 2
TILES = (T0, T12, T12)

KINDS = ("PWPW", "PVPWPPPWPV", "WPVPPPWPPV")
STEP = [(l, g, KINDS[l][g]) for l in (1, 0, 2) for g in range(len(KINDS[l]))]
FIRST_STEP = [e for e in STEP if e[0] == 0]
LAST_STEP = [e for e in STEP if e[0] != 0]
WHOLE_RING, RAW_RING, PSUM_RING, HI_RING, LO_RING = 4, 4, 2, 6, 4
TWICE = 4
SUMS_AT = (2, 2)
V_LAG = 2
RELU2_AT = (1, 4)
RELU0_AT = (2, 4)


assert KINDS[1][-1] == KINDS[2][-1] == "V"


def tiles_of(layer, g):
    return range(G * g, min(G * g + G, TILES[layer]))


def rows_of(layer, t):
    if layer == 0:
        return P0 if t < T0 - 1 else P0_LAST
    return 128


def weight_places():
    place, n = {}, {"split": T0, "whole": 0}
    for layer, g, kind in STEP:
        for t in tiles_of(layer, g):
            if layer == 0:
                place[layer, t] = t
            elif kind != "W":
                place[layer, t] = n["split"]
                n["split"] += 1
            else:
                place[layer, t] = n["whole"]
                n["whole"] += 1
    return place, n["split"], n["whole"]


PLACE, N_SPLIT, N_WHOLE = weight_places()


def cin(nc, x2, w0a, w0b, w1, w2, w_rest, b, out):
    with ExitStack() as ctx:
        def sb(name, shape, dt=F32):
            return ctx.enter_context(nc.sbuf_tensor(name, shape, dt))

        def psum(name, shape):
            return ctx.enter_context(nc.psum_tensor(name, shape, F32))

        def sem(name):
            return ctx.enter_context(nc.semaphore(name))

        w0 = sb("w0", [P0, T0, SIZE])
        w_whole = sb("w_whole", [128, N_WHOLE, SIZE])
        w_hi = sb("w_hi", [128, N_SPLIT, SIZE], F32R)
        w_lo = sb("w_lo", [128, N_SPLIT, SIZE], F32R)
        bias = sb("bias", [128, 3])
        xrep = sb("xrep", [P0, N])
        xshift = sb("xshift", [P0, T0, N])
        G12 = len(KINDS[1])
        xwide2 = sb("xwide2", [128, 2, G * TWICE, N])
        xwide1 = sb("xwide1", [128, T12 - G * TWICE, N])
        z_whole = sb("z_whole", [128, WHOLE_RING, G, N])
        z_raw = sb("z_raw", [128, RAW_RING, G, N])
        z_hi = sb("z_hi", [128, HI_RING, G, N], F32R)
        z_lo = sb("z_lo", [128, LO_RING, G, N], F32R)
        direct = sb("direct", [128, 2, N])
        last = sb("last", [128, N])
        sums01 = sb("sums01", [128, BATCH])
        sums2 = sb("sums2", [128, BATCH])
        acc = psum("acc", [128, 2, N])
        h = [psum("h0", [128, N]), psum("h1", [128, N])]
        z_psum = psum("z_psum", [128, PSUM_RING, G, N])
        stage = [None, xwide2[:, 1, 0:4, :].rearrange("p a (b s) -> p (a b) s", s=SIZE),
                 xwide2[:, 1, 4:8, :].rearrange("p a (b s) -> p (a b) s", s=SIZE)]
        w0t = direct[:].rearrange("p a (b s) -> p (a b) s", s=SIZE)[0:P0, 0:T0, :]

        w0_in = sem("w0_in")
        w0_folded = sem("w0_folded")
        w_staged = [None, sem("w1_staged"), sem("w2_staged")]
        w_whole_in = sem("w_whole_in")
        w_hi_made = sem("w_hi_made")
        w_lo_made = sem("w_lo_made")
        w1_lo_made = sem("w1_lo_made")
        bias_in = sem("bias_in")
        xs_in = sem("xs_in")
        xw2_in = [[sem(f"xw_in{p}_{g}") for g in range(TWICE)] for p in range(2)]
        xw1_in = {g: sem(f"xw_in_{g}") for g in range(TWICE, G12)}
        made = {k: sem(f"z_made_{k}") for k in "WPV"}
        hi_made = sem("hi_made")
        lo_made = {"P": sem("lo_made_P"), "V": sem("lo_made_V")}
        whole_used = sem("whole_used")
        split_used = sem("split_used")
        h_ready = [sem("h0_ready"), sem("h1_ready")]
        acc_read = [sem(f"acc_read{l}") for l in range(3)]
        summed = sem("summed")
        out_sent = sem("out_sent")

        def order(j):
            if isinstance(j, int) and j in (-1, BLOCKS - 1):
                return FIRST_STEP if j < 0 else LAST_STEP
            return STEP

        def before(kinds, j, pos):
            here = sum(e[2] in kinds for e in order(j)[:pos])
            if isinstance(j, int) and j < 0:
                return here
            return sum(e[2] in kinds for e in FIRST_STEP) + j * sum(e[2] in kinds for e in STEP) + here

        def slot(kinds, pair, par, pos, ring):
            j = 2 * pair + par
            return before(kinds, j if isinstance(j, int) else par, pos) % ring

        for kinds, ring in (("W", WHOLE_RING), ("P", RAW_RING), ("V", PSUM_RING), ("PV", HI_RING), ("PV", LO_RING)):
            assert 2 * sum(e[2] in kinds for e in STEP) % ring == 0

        def place_of(j, layer, g):
            return [e[:2] for e in order(j)].index((layer, g))

        def acc_of(layer, pair, par):
            return acc[:, par if layer == 0 else 1 - par, :]

        def ready(eng, semaphore, value, needed=0):
            if not isinstance(value, int) or value > 0:
                eng.wait_ge(semaphore, value)

        def take(eng, z, hi, lo, layer, g):
            n = len(tiles_of(layer, g))
            rows = P0 if layer == 0 else 128
            if layer and g == G12 - 1:
                under = slice(HALF, 128)
                eng.tensor_tensor(lo[:, 0:n - 1, :], z[:, 0:n - 1, :], hi[:, 0:n - 1, :].bitcast(F32), ALU.subtract)
                return eng.tensor_tensor(hi[under, n - 1, :], z[under, n - 1, :], hi[under, n - 1, :].bitcast(F32),
                                         ALU.subtract)
            return eng.tensor_tensor(lo[0:rows, 0:n, :], z[0:rows, 0:n, :], hi[0:rows, 0:n, :].bitcast(F32),
                                     ALU.subtract)

        block = ctx.enter_context(nc.Block())

        @block.sync
        def _(sp):
            def load_shifted(j):
                for a in range(PER):
                    rows = slice(a * FIELDS, (a + 1) * FIELDS)
                    sp.dma_start(xrep[rows, :], x2[0:FIELDS, bass.ds(N * j, N)]).then_inc(xs_in, 16)
                    src = bass.AP(x2.tensor, x2.offset + COLS * a + N * j,
                                  [[COLS, FIELDS], [PER * COLS, T0], [1, N]])
                    sp.dma_start(xshift[rows, :, :], src).then_inc(xs_in, 16)

            def load_wide(dst, landed, j, g):
                for e in range(2):
                    first, apart = (2 * G * g + e, 2) if (g, e) != (G12 - 1, 1) else (FIELDS - 2, 1)
                    src = bass.AP(x2.tensor, x2.offset + COLS * first + N * j,
                                  [[0, HALF], [apart * COLS, G], [1, N]])
                    sp.dma_start(dst[HALF * e:HALF * (e + 1), :, :], src).then_inc(landed, 16)

            def load_twice(j, par, g):
                load_wide(xwide2[:, par, G * g:G * (g + 1), :], xw2_in[par][g], j, g)

            def load_once(j, g):
                load_wide(xwide1[:, G * (g - TWICE):G * (g + 1 - TWICE), :], xw1_in[g], j, g)

            def refill(pair, par, far=True):
                j = 2 * pair + par
                if far:
                    pos = place_of(j, 0, len(KINDS[0]) - 1)
                    kind = order(j)[pos][2]
                    sp.wait_ge(made[kind], before(kind, j, pos) + 1)
                    load_shifted(j + 2)
                for g in range(G12):
                    if g < TWICE and not far:
                        continue
                    pos = place_of(j, 2, g)
                    kind = order(j)[pos][2]
                    sp.wait_ge(made[kind], before(kind, j, pos) + 1)
                    if g < TWICE:
                        load_twice(j + 2, par, g)
                    else:
                        load_once(j + 1, g)

            sp.dma_start(w0[:], w0a).then_inc(w0_in, 16)
            sp.dma_start(w0t, w0b).then_inc(w0_in, 16)
            load_shifted(0)
            sp.dma_start(bias[:], b).then_inc(bias_in, 16)
            sp.dma_start(stage[1][:, 0:SPLIT_COUNT[1], :], w1).then_inc(w_staged[1], 16)
            for g in range(G12):
                if g < TWICE:
                    load_twice(0, 0, g)
                else:
                    load_once(0, g)
                if g == 1:
                    sp.dma_start(w_whole[:], w_rest).then_inc(w_whole_in, 16)
            sp.dma_start(stage[2][:, 0:SPLIT_COUNT[2], :], w2).then_inc(w_staged[2], 16)
            ready(sp, made[KINDS[0][-1]], before(KINDS[0][-1], -1, len(KINDS[0])))
            load_shifted(1)
            sp.wait_ge(w_lo_made, 2)
            sp.wait_ge(w1_lo_made, 1)
            for g in range(TWICE):
                load_twice(1, 1, g)
            with sp.Fori(0, PAIRS - 1) as pair:
                for par in range(2):
                    refill(pair, par)
            refill(PAIRS - 1, 0, far=False)
            done = BATCH - BB
            sp.wait_ge(summed, 2 * BLOCKS - 1)
            sp.dma_start(out[0:HALF, :], sums01[HALF:SIZE, :]).then_inc(out_sent, 16)
            sp.dma_start(out[HALF:SIZE, :], sums01[0:HALF, :]).then_inc(out_sent, 16)
            sp.dma_start(out[SIZE:2 * SIZE, 0:done], sums2[:, 0:done]).then_inc(out_sent, 16)
            sp.wait_ge(summed, 2 * BLOCKS)
            sp.dma_start(out[SIZE:2 * SIZE, done:BATCH], sums2[:, done:BATCH]).then_inc(out_sent, 16)
            sp.wait_ge(out_sent, 64)

        @block.vector
        def _(dve):
            def products(pair, par, pos):
                j = 2 * pair + par
                layer, g, kind = order(j)[pos]
                n = len(tiles_of(layer, g))
                rows = P0 if layer == 0 else 128
                if layer == 0:
                    if g == 0:
                        dve.wait_ge(xs_in, 32 * PER * (j + 2))
                    in0 = xrep[:, None, :].to_broadcast([P0, n, N])
                    in1 = xshift[:, G * g:G * g + n, :]
                else:
                    if g == 0:
                        dve.wait_ge(h_ready[layer - 1], 2 * (j + 1))
                    in0 = h[layer - 1][:, None, :].to_broadcast([128, n, N])
                    if g < TWICE:
                        in1 = xwide2[:, par, G * g:G * g + n, :]
                        if layer == 1:
                            dve.wait_ge(xw2_in[par][g], 32 * (pair + 1))
                    else:
                        in1 = xwide1[:, G * (g - TWICE):G * (g - TWICE) + n, :]
                        if layer == 1:
                            dve.wait_ge(xw1_in[g], 32 * (j + 1))
                number = before(kind, j, pos)
                if kind == "W":
                    ready(dve, whole_used, number - WHOLE_RING + 1)
                    dst = z_whole[0:rows, slot("W", pair, par, pos, WHOLE_RING), 0:n, :]
                elif kind == "P":
                    ready(dve, lo_made["P"], number - RAW_RING + 1)
                    dst = z_raw[0:rows, slot("P", pair, par, pos, RAW_RING), 0:n, :]
                else:
                    ready(dve, lo_made["V"], number - PSUM_RING + 1)
                    dst = z_psum[0:rows, slot("V", pair, par, pos, PSUM_RING), 0:n, :]
                nc.vector.tensor_tensor(dst, in0, in1, ALU.mult).then_inc(made[kind], 1)

            def subtract(pair, par, pos):
                j = 2 * pair + par
                layer, g, _ = order(j)[pos]
                number = before("PV", j, pos)
                dve.wait_ge(hi_made, number + 1)
                ready(dve, split_used, number - LO_RING + 1)
                take(nc.vector, z_psum[:, slot("V", pair, par, pos, PSUM_RING)],
                     z_hi[:, slot("PV", pair, par, pos, HI_RING)],
                     z_lo[:, slot("PV", pair, par, pos, LO_RING)], layer, g).then_inc(lo_made["V"], 1)

            def sum_direct(j, par):
                dve.wait_ge(acc_read[1], j + 1)
                nc.vector.tensor_reduce(sums01[:, bass.ds(BB * j, BB)],
                                        direct[:, par, :].rearrange("p (b d) -> p b d", d=DIM),
                                        AX_X, ALU.add).then_inc(summed, 1)

            def sum_last(j):
                dve.wait_ge(acc_read[2], j + 1)
                nc.vector.tensor_reduce(sums2[:, bass.ds(BB * j, BB)],
                                        last[:].rearrange("p (b d) -> p b d", d=DIM),
                                        AX_X, ALU.add).then_inc(summed, 1)

            def step(pair, par):
                j = 2 * pair + par
                late = [(V_LAG - 1, pair + par - 1, 1 - par, len(STEP) - 1)]
                if isinstance(j, int) and j == 0:
                    late = []
                for pos, (layer, g, kind) in enumerate(order(j)):
                    if (layer, g) == (2, 0):
                        while late:
                            subtract(*late.pop(0)[1:])
                    products(pair, par, pos)
                    while late and pos >= late[0][0]:
                        subtract(*late.pop(0)[1:])
                    if kind == "V":
                        late.append((pos + V_LAG, pair, par, pos))
                    if (layer, g) == SUMS_AT:
                        sum_direct(j, par)
                        if not isinstance(j, int) or j > 0:
                            sum_last(j - 1)
                assert [p[3] for p in late] == [len(order(j)) - 1]

            dve.wait_ge(w0_in, 32)
            nc.vector.tensor_tensor(w0[:], w0[:], w0t, ALU.add).then_inc(w0_folded, 1)
            for pos in range(len(FIRST_STEP)):
                products(-1, 1, pos)
            a, n = SPLIT_FROM[1], SPLIT_COUNT[1]
            dve.wait_ge(w_hi_made, 2)
            nc.vector.tensor_tensor(w_lo[:, a:a + n, :], stage[1][:, 0:n, :], w_hi[:, a:a + n, :].bitcast(F32),
                                    ALU.subtract).then_inc(w1_lo_made, 1)
            step(0, 0)
            step(0, 1)
            with dve.Fori(1, PAIRS - 1) as pair:
                for par in range(2):
                    step(pair, par)
            step(PAIRS - 1, 0)
            step(PAIRS - 1, 1)
            subtract(PAIRS - 1, 1, len(LAST_STEP) - 1)
            sum_last(BLOCKS - 1)

        @block.gpsimd
        def _(pool):
            def subtract(pair, par, pos):
                j = 2 * pair + par
                layer, g, _ = order(j)[pos]
                number = before("PV", j, pos)
                pool.wait_ge(hi_made, number + 1)
                ready(pool, split_used, number - LO_RING + 1)
                take(nc.gpsimd, z_raw[:, slot("P", pair, par, pos, RAW_RING)],
                     z_hi[:, slot("PV", pair, par, pos, HI_RING)],
                     z_lo[:, slot("PV", pair, par, pos, LO_RING)], layer, g).then_inc(lo_made["P"], 1)

            def step(pair, par):
                j = 2 * pair + par
                for pos, (layer, g, kind) in enumerate(order(j)):
                    if (layer, g) == (0, 0) and isinstance(j, int) and j == 0:
                        split(2, stage[2][:, 0:SPLIT_COUNT[2], :], 128)
                    if kind == "P":
                        subtract(pair, par, pos)

            def split(layer, raw, rows):
                a, n = SPLIT_FROM[layer], SPLIT_COUNT[layer]
                pool.wait_ge(w_hi_made, layer + 1)
                nc.gpsimd.tensor_tensor(w_lo[0:rows, a:a + n, :], raw, w_hi[0:rows, a:a + n, :].bitcast(F32),
                                        ALU.subtract).then_inc(w_lo_made, 1)

            split(0, w0[:, 0:SPLIT_COUNT[0], :], P0)
            step(-1, 1)
            step(0, 0)
            step(0, 1)
            with pool.Fori(1, PAIRS - 1) as pair:
                for par in range(2):
                    step(pair, par)
            step(PAIRS - 1, 0)
            step(PAIRS - 1, 1)

        @block.tensor
        def _(pe):
            def contract(pair, par, pos):
                j = 2 * pair + par
                layer, g, kind = order(j)[pos]
                ts = tiles_of(layer, g)
                last_g = g == len(KINDS[layer]) - 1
                dst = acc_of(layer, pair, par)
                number = before(kind, j, pos)

                def matmul(w, z, t, first, final):
                    rows = rows_of(layer, t)
                    return nc.tensor.matmul(dst, w[0:rows, PLACE[layer, t], :], z[0:rows, t - G * g, :],
                                            start=first and t == 0,
                                            stop=final and t == TILES[layer] - 1)

                if g == 0 and layer == 1:
                    pe.wait_ge(acc_read[0], j + 1)
                elif g == 0 and layer == 2:
                    if isinstance(j, int) and j == 0:
                        pe.wait_ge(w_lo_made, 2)
                    pe.wait_ge(acc_read[1], j + 1)
                elif g == 0:
                    ready(pe, acc_read[2], j)
                if kind == "W":
                    pe.wait_ge(made["W"], number + 1)
                    z = z_whole[:, slot("W", pair, par, pos, WHOLE_RING)]
                    for t in ts:
                        mm = matmul(w0 if layer == 0 else w_whole, z, t, True, True)
                    mm.then_inc(whole_used, 1)
                    return
                pe.wait_ge(hi_made, before("PV", j, pos) + 1)
                hi = z_hi[:, slot("PV", pair, par, pos, HI_RING)]
                stacked = ts[-1] if layer and last_g else None
                ts = [t for t in ts if t != stacked]
                for t in ts:
                    matmul(w_hi, hi, t, True, False)
                for t in ts:
                    matmul(w_lo, hi, t, False, False)
                pe.wait_ge(lo_made[kind], number + 1)
                lo = z_lo[:, slot("PV", pair, par, pos, LO_RING)]
                for t in ts:
                    mm = matmul(w_hi, lo, t, False, stacked is None)
                if stacked is not None:
                    matmul(w_hi, hi, stacked, False, False)
                    mm = matmul(w_lo, hi, stacked, False, True)
                mm.then_inc(split_used, 1)

            def step(pair, par):
                for pos in range(len(order(2 * pair + par))):
                    contract(pair, par, pos)

            pe.wait_ge(w0_folded, 1)
            pe.wait_ge(w_lo_made, 1)
            step(-1, 1)
            pe.wait_ge(w_whole_in, 16)
            pe.wait_ge(w1_lo_made, 1)
            step(0, 0)
            step(0, 1)
            with pe.Fori(1, PAIRS - 1) as pair:
                for par in range(2):
                    step(pair, par)
            step(PAIRS - 1, 0)
            step(PAIRS - 1, 1)

        @block.scalar
        def _(act):
            def high_part(pair, par, pos):
                j = 2 * pair + par
                layer, g, kind = order(j)[pos]
                n = len(tiles_of(layer, g))
                rows = P0 if layer == 0 else 128
                act.wait_ge(made[kind], before(kind, j, pos) + 1)
                ready(act, split_used, before("PV", j, pos) - HI_RING + 1)
                if kind == "P":
                    src = z_raw[0:rows, slot("P", pair, par, pos, RAW_RING), 0:n, :]
                else:
                    src = z_psum[0:rows, slot("V", pair, par, pos, PSUM_RING), 0:n, :]
                nc.scalar.copy(z_hi[0:rows, slot("PV", pair, par, pos, HI_RING), 0:n, :], src).then_inc(hi_made, 1)

            def relu(dst, src, layer, rows):
                return nc.scalar.activation(dst, src, ACT.Relu, bias=bias[rows, layer:layer + 1])

            def wait_acc(layer, j, step_j):
                pos = place_of(step_j, layer, len(KINDS[layer]) - 1)
                if KINDS[layer][-1] == "W":
                    act.wait_ge(whole_used, before("W", step_j, pos) + 1)
                else:
                    act.wait_ge(split_used, before("PV", step_j, pos) + 1)

            def relu0(pair, par):
                j = 2 * pair + par
                wait_acc(0, j + 1, j)
                a = acc_of(0, pair, par)
                relu(h[0][0:HALF, :], a[0:HALF, :], 0, slice(0, HALF)).then_inc(h_ready[0], 1)
                relu(h[0][HALF:, :], a[0:HALF, :], 0, slice(0, HALF)).then_inc(h_ready[0], 1)
                relu(direct[HALF:, 1 - par, :], a[HALF:, :], 0, slice(HALF, SIZE)).then_inc(acc_read[0], 1)

            def relu1(pair, par):
                j = 2 * pair + par
                wait_acc(1, j, j)
                a = acc_of(1, pair, par)
                relu(h[1][0:HALF, :], a[HALF:, :], 1, slice(HALF, SIZE)).then_inc(h_ready[1], 1)
                relu(h[1][HALF:, :], a[HALF:, :], 1, slice(HALF, SIZE)).then_inc(h_ready[1], 1)
                relu(direct[0:HALF, par, :], a[0:HALF, :], 1, slice(0, HALF)).then_inc(acc_read[1], 1)

            def relu2(pair, par):
                j = 2 * pair + par
                wait_acc(2, j, j)
                relu(last[:], acc_of(2, pair, par), 2, slice(0, SIZE)).then_inc(acc_read[2], 1)

            def step(pair, par):
                j = 2 * pair + par
                for pos, (layer, g, kind) in enumerate(order(j)):
                    if (layer, g) == RELU2_AT and not (isinstance(j, int) and j == 0):
                        relu2(pair + par - 1, 1 - par)
                    if (layer, g) == (0, 0) and isinstance(j, int) and j == 0:
                        split_layer(2)
                    if (layer, g) == (2, 0):
                        relu1(pair, par)
                    if (layer, g) == RELU0_AT and not (isinstance(j, int) and j == BLOCKS - 1):
                        relu0(pair, par)
                    if kind != "W":
                        high_part(pair, par, pos)

            def split(layer, raw, a, n, rows):
                nc.scalar.copy(w_hi[0:rows, a:a + n, :], raw).then_inc(w_hi_made, 1)

            def split_layer(layer):
                act.wait_ge(w_staged[layer], 16)
                split(layer, stage[layer][:, 0:SPLIT_COUNT[layer], :], SPLIT_FROM[layer],
                      SPLIT_COUNT[layer], 128)

            act.wait_ge(w0_folded, 1)
            split(0, w0[:, 0:SPLIT_COUNT[0], :], SPLIT_FROM[0], SPLIT_COUNT[0], P0)
            for pos, (_, _, kind) in enumerate(FIRST_STEP):
                if kind != "W":
                    high_part(-1, 1, pos)
            split_layer(1)
            act.wait_ge(bias_in, 16)
            relu0(-1, 1)
            step(0, 0)
            step(0, 1)
            with act.Fori(1, PAIRS - 1) as pair:
                for par in range(2):
                    step(pair, par)
            step(PAIRS - 1, 0)
            step(PAIRS - 1, 1)
            relu2(PAIRS - 1, 1)


SPLIT_FROM = [min([PLACE[l, t] for _l, g, k in STEP if _l == l and k != "W" for t in tiles_of(l, g)]) for l in range(3)]
SPLIT_COUNT = [T0] + [sum(len(tiles_of(l, g)) for _l, g, k in STEP if _l == l and k != "W") for l in (1, 2)]

def kernel(r_x, L0_rec_W0, L0_rec_W1, L0_rec_W2, L0_rec_b0, L0_rec_b1, L0_rec_b2):
    import numpy as np
    import concourse.bacc as bacc
    from concourse.bass_utils import run_bass_kernel_spmd

    x = np.asarray(r_x).transpose(1, 0, 2).reshape(FIELDS, COLS)
    w0 = np.asarray(L0_rec_W0).reshape(FIELDS, FIELDS, SIZE)
    w0a = np.zeros((PER, FIELDS, T0, SIZE), np.float32)
    w0b = np.zeros((PER, FIELDS, T0, SIZE), np.float32)
    f = np.arange(FIELDS)
    for s in range(SHIFTS):
        g = (f + s) % FIELDS
        w0a[s % PER, :, s // PER] = w0[f, g]
        if s:
            w0b[s % PER, :, s // PER] = w0[g, f]

    def tiled(w):
        w = np.concatenate([w, w[-HALF:]])
        return w.reshape(T12, 128, SIZE).transpose(1, 0, 2)

    def some(w, layer, whole):
        return w[:, [t for g, k in enumerate(KINDS[layer]) if (k == "W") == whole for t in tiles_of(layer, g)]]

    def swapped(w):
        return np.concatenate([w[..., HALF:], w[..., :HALF]], axis=-1)

    w1 = tiled(swapped(np.asarray(L0_rec_W1)))
    w2 = tiled(np.asarray(L0_rec_W2))
    arrays = {
        "x2": np.concatenate([x, x]),
        "w0a": w0a.reshape(P0, T0, SIZE),
        "w0b": w0b.reshape(P0, T0, SIZE),
        "w1": some(w1, 1, False),
        "w2": some(w2, 2, False),
        "w_rest": np.concatenate([some(w1, 1, True), some(w2, 2, True)], axis=1),
        "b": np.stack([np.asarray(L0_rec_b0), swapped(np.asarray(L0_rec_b1)), np.asarray(L0_rec_b2)], axis=1),
    }
    arrays = {k: np.ascontiguousarray(v) for k, v in arrays.items()}
    nc = bacc.Bacc("TRN2", target_bir_lowering=False, num_devices=1)
    args = [nc.dram_tensor(k, v.shape, F32, kind="ExternalInput").ap() for k, v in arrays.items()]
    out = nc.dram_tensor("out", (2 * SIZE, BATCH), F32, kind="ExternalOutput").ap()
    cin(nc, *args, out)
    r = run_bass_kernel_spmd(nc, [arrays], core_ids=[0])
    return np.ascontiguousarray(r.results[0]["out"].T)
```

```python
from contextlib import ExitStack

import concourse.bass as bass
from concourse import mybir

F32 = mybir.dt.float32
F32R = mybir.dt.float32r
ALU = mybir.AluOpType
ACT = mybir.ActivationFunctionType
AX_X = mybir.AxisListType.X

FIELDS = 39
DIM = 16
BATCH = 512
SIZE = 128
HALF = SIZE // 2
COLS = BATCH * DIM
N = 512
BLOCKS = COLS // N
PAIRS = BLOCKS // 2
BB = N // DIM

SHIFTS = FIELDS // 2 + 1
PER = 3
T0 = -(-SHIFTS // PER)
P0 = PER * FIELDS
P0_LAST = (SHIFTS - PER * (T0 - 1)) * FIELDS
T12 = -(-FIELDS // 2)
G = 2
TILES = (T0, T12, T12)

KINDS = ("WPWP", "PWPWPPVPPV", "PPWPVPPWPV") 
G12 = len(KINDS[1])
SCHEDULE = "111112100122221001212222"
WHOLE_RING, RAW_RING, HI_RING, LO_RING = 4, 4, 6, 4 
V_LAG = 2
XREP_AT = 5
RELU0_AT = 21
RELU1_AT = 0
RELU2_AT = 3
SUM1_AT = 7
SUM2_AT = 8

assert KINDS[1][-1] == KINDS[2][-1] == "V"


def steps():
    seen, full = [0, 0, 0], []
    for c in SCHEDULE:
        layer = int(c)
        full.append((layer, seen[layer], KINDS[layer][seen[layer]]))
        seen[layer] += 1
    assert seen == [len(k) for k in KINDS]
    return full


STEP = steps()


def order(j):
    if isinstance(j, int):
        return [e for e in STEP if 0 <= j + (1, 0, -1)[e[0]] < BLOCKS]
    return STEP


def before(kinds, j, pos):
    here = sum(e[2] in kinds for e in order(j)[:pos])
    if isinstance(j, int):
        return here + sum(e[2] in kinds for i in range(-1, j) for e in order(i))
    return before(kinds, 1, 0) + (j - 1) * sum(e[2] in kinds for e in STEP) + here


def tiles_of(layer, g):
    return range(G * g, min(G * g + G, TILES[layer]))


def rows_of(layer, t):
    if layer == 0:
        return P0 if t < T0 - 1 else P0_LAST
    return 128


def weight_places():
    place, n = {}, {"split": 0, "whole": 0}
    for layer, g, kind in sorted(STEP):
        for t in tiles_of(layer, g):
            if kind != "W":
                place[layer, t] = n["split"]
                n["split"] += 1
            elif layer:
                place[layer, t] = n["whole"]
                n["whole"] += 1
            else:
                place[layer, t] = t
    return place, n["split"], n["whole"]


PLACE, N_SPLIT, N_WHOLE = weight_places()
SPLIT_TILES = [[t for l, g, k in sorted(STEP) if l == layer and k != "W" for t in tiles_of(l, g)]
               for layer in range(3)]
SPLIT_FROM = [PLACE[layer, ts[0]] for layer, ts in enumerate(SPLIT_TILES)]
SPLIT_COUNT = [len(ts) for ts in SPLIT_TILES]
SPLIT0 = [(PLACE[0, tiles_of(0, g)[0]], tiles_of(0, g)) for g, k in enumerate(KINDS[0]) if k != "W"]
SPLIT2_BEFORE = (1, 9)
assert len(SPLIT0) > 0 and SPLIT_COUNT[1] <= 16 and SPLIT_COUNT[2] <= 16


def cin(nc, x2, w0a, w0b, w1, w2, w_rest, b, out):
    with ExitStack() as ctx:
        def sb(name, shape, dt=F32):
            return ctx.enter_context(nc.sbuf_tensor(name, shape, dt))

        def psum(name, shape):
            return ctx.enter_context(nc.psum_tensor(name, shape, F32))

        def sem(name):
            return ctx.enter_context(nc.semaphore(name))

        w0 = sb("w0", [P0, T0, SIZE])
        w_whole = sb("w_whole", [128, N_WHOLE, SIZE])
        w_hi = sb("w_hi", [128, N_SPLIT, SIZE], F32R)
        w_lo = sb("w_lo", [128, N_SPLIT, SIZE], F32R)
        bias = sb("bias", [128, 3])
        xrep = sb("xrep", [P0, N])
        xshift = sb("xshift", [P0, T0, N])
        xwide = sb("xwide", [128, 2, T12, N])
        z_whole = sb("z_whole", [128, WHOLE_RING, G, N])
        z_raw = sb("z_raw", [128, RAW_RING, G, N])
        z_hi = sb("z_hi", [128, HI_RING, G, N], F32R)
        z_lo = sb("z_lo", [128, LO_RING, G, N], F32R)
        direct = sb("direct", [128, 2, N])
        last = sb("last", [128, N])
        sums01 = sb("sums01", [128, BATCH])
        sums2 = sb("sums2", [128, BATCH])
        acc = [psum(f"acc{l}", [128, N]) for l in range(3)]
        h = [psum("h0", [128, N]), psum("h1", [128, N])]
        xrep_psum = psum("xrep_psum", [128, N])
        z_psum = psum("z_psum", [128, G, N])
        stage = [None, xwide[:, 1, T12 - 4:T12, :].rearrange("p a (b s) -> p (a b) s", s=SIZE),
                 xwide[:, 1, T12 - 8:T12 - 4, :].rearrange("p a (b s) -> p (a b) s", s=SIZE)]
        w0t = direct[:].rearrange("p a (b s) -> p (a b) s", s=SIZE)[0:P0, 0:T0, :]

        w0_in = sem("w0_in")
        w0_folded = sem("w0_folded")
        w_staged = [None, sem("w1_staged"), sem("w2_staged")]
        w_whole_in = sem("w_whole_in")
        w_hi_made = sem("w_hi_made")
        w_lo_made = sem("w_lo_made")
        w1_lo_made = sem("w1_lo_made")
        bias_in = sem("bias_in")
        xrep_in = sem("xrep_in")
        xshift_in = sem("xshift_in")
        xshift_first_in = sem("xshift_first_in")
        xw_in = [[sem(f"xw_in{p}_{g}") for g in range(G12)] for p in range(2)]
        made = {k: sem(f"z_made_{k}") for k in "WPV"}
        hi_made = sem("hi_made")
        lo_made = {"P": sem("lo_made_P"), "V": sem("lo_made_V")}
        whole_used = sem("whole_used")
        split_used = sem("split_used")
        xrep_ready = sem("xrep_ready")
        h_ready = [sem("h0_ready"), sem("h1_ready")]
        acc_read = [sem(f"acc_read{l}") for l in range(3)]
        summed = sem("summed")
        out_sent = sem("out_sent")

        def step_of(pair, par):
            return 2 * pair + 1 + par

        def slot(kinds, pair, par, pos, ring):
            j = step_of(pair, par)
            return before(kinds, j if isinstance(j, int) else 1 + par, pos) % ring

        for kinds, ring in (("W", WHOLE_RING), ("P", RAW_RING), ("PV", HI_RING), ("PV", LO_RING)):
            assert 2 * sum(e[2] in kinds for e in STEP) % ring == 0

        def place_of(j, layer):
            return [e[:2] for e in order(j)].index((layer, len(KINDS[layer]) - 1))

        def made_all(j, layer):
            kind = KINDS[layer][-1]
            return made[kind], before(kind, j, place_of(j, layer)) + 1

        def ready(eng, semaphore, value):
            if not isinstance(value, int) or value > 0:
                eng.wait_ge(semaphore, value)

        def take(eng, z, hi, lo, layer, g):
            n = len(tiles_of(layer, g))
            rows = P0 if layer == 0 else 128
            if layer and g == G12 - 1:
                under = slice(HALF, 128)
                eng.tensor_tensor(lo[:, 0:n - 1, :], z[:, 0:n - 1, :], hi[:, 0:n - 1, :].bitcast(F32), ALU.subtract)
                return eng.tensor_tensor(hi[under, n - 1, :], z[under, n - 1, :], hi[under, n - 1, :].bitcast(F32),
                                         ALU.subtract)
            return eng.tensor_tensor(lo[0:rows, 0:n, :], z[0:rows, 0:n, :], hi[0:rows, 0:n, :].bitcast(F32),
                                     ALU.subtract)

        block = ctx.enter_context(nc.Block())

        @block.sync
        def _(sp):
            def load_rep(j):
                for a in range(PER):
                    sp.dma_start(xrep[a * FIELDS:(a + 1) * FIELDS, :],
                                 x2[0:FIELDS, bass.ds(N * j, N)]).then_inc(xrep_in, 16)

            def load_shift(j, landed, ts=range(T0)):
                for a in range(PER):
                    src = bass.AP(x2.tensor, x2.offset + COLS * (PER * ts[0] + a) + N * j,
                                  [[COLS, FIELDS], [PER * COLS, len(ts)], [1, N]])
                    sp.dma_start(xshift[a * FIELDS:(a + 1) * FIELDS, ts[0]:ts[-1] + 1, :], src).then_inc(landed, 16)

            def load_wide(j, half, g):
                for e in range(2):
                    first, apart = (2 * G * g + e, 2) if (g, e) != (G12 - 1, 1) else (FIELDS - 2, 1)
                    src = bass.AP(x2.tensor, x2.offset + COLS * first + N * j,
                                  [[0, HALF], [apart * COLS, G], [1, N]])
                    sp.dma_start(xwide[HALF * e:HALF * (e + 1), half, G * g:G * (g + 1), :],
                                 src).then_inc(xw_in[half][g], 16)

            def refill(pair, par):
                j = step_of(pair, par)
                for pos, (layer, g, kind) in enumerate(order(j)):
                    if layer == 0 and g == len(KINDS[0]) - 1 and not (isinstance(j, int) and j + 2 >= BLOCKS):
                        sp.wait_ge(*made_all(j, 0))
                        load_rep(j + 2)
                        load_shift(j + 2, xshift_in)
                    if layer == 2 and not (isinstance(j, int) and j + 1 >= BLOCKS):
                        sp.wait_ge(made[kind], before(kind, j, pos) + 1)
                        load_wide(j + 1, par, g)

            sp.dma_start(w0[:], w0a).then_inc(w0_in, 16)
            sp.dma_start(w0t, w0b).then_inc(w0_in, 16)
            load_rep(0)
            load_shift(0, xshift_first_in, range(0, 2 * G))
            load_shift(0, xshift_in, range(2 * G, T0))
            sp.dma_start(bias[:], b).then_inc(bias_in, 16)
            sp.dma_start(stage[1][:, 0:SPLIT_COUNT[1], :], w1).then_inc(w_staged[1], 16)
            for g in range(G12):
                load_wide(0, 0, g)
                if g == 1:
                    sp.dma_start(w_whole[:], w_rest).then_inc(w_whole_in, 16)
                if g == 5:
                    sp.wait_ge(*made_all(-1, 0))
                    load_rep(1)
                    load_shift(1, xshift_in)
            sp.dma_start(stage[2][:, 0:SPLIT_COUNT[2], :], w2).then_inc(w_staged[2], 16)
            for g in range(G12):
                if g == G12 - 4:
                    sp.wait_ge(w1_lo_made, 1)
                    sp.wait_ge(w_lo_made, len(SPLIT0) + 1)
                load_wide(1, 1, g)
            refill(-1, 1)
            with sp.Fori(0, PAIRS - 2) as pair:
                for par in range(2):
                    refill(pair, par)
            for par in range(2):
                refill(PAIRS - 2, par)
            done = BATCH - BB
            sp.wait_ge(summed, 2 * BLOCKS - 1)
            sp.dma_start(out[0:HALF, :], sums01[HALF:SIZE, :]).then_inc(out_sent, 16)
            sp.dma_start(out[HALF:SIZE, :], sums01[0:HALF, :]).then_inc(out_sent, 16)
            sp.dma_start(out[SIZE:2 * SIZE, 0:done], sums2[:, 0:done]).then_inc(out_sent, 16)
            sp.wait_ge(summed, 2 * BLOCKS)
            sp.dma_start(out[SIZE:2 * SIZE, done:BATCH], sums2[:, done:BATCH]).then_inc(out_sent, 16)
            sp.wait_ge(out_sent, 64)

        @block.vector
        def _(dve):
            def products(pair, par, pos):
                j = step_of(pair, par)
                layer, g, kind = order(j)[pos]
                n = len(tiles_of(layer, g))
                rows = P0 if layer == 0 else 128
                if layer == 0:
                    first = isinstance(j, int) and j == -1
                    if g == 0:
                        dve.wait_ge(xrep_ready, j + 2)
                    if first and g == 0:
                        dve.wait_ge(xshift_first_in, 16 * PER)
                    elif g == (2 if first else 0):
                        dve.wait_ge(xshift_in, 16 * PER * (j + 2))
                    in0 = xrep_psum[0:P0, None, :].to_broadcast([P0, n, N])
                    in1 = xshift[:, G * g:G * g + n, :]
                elif layer == 1:
                    if g == 0:
                        dve.wait_ge(h_ready[0], 2 * (j + 1))
                    dve.wait_ge(xw_in[1 - par][g], 32 * (pair + par + 1))
                    in0 = h[0][:, None, :].to_broadcast([128, n, N])
                    in1 = xwide[:, 1 - par, G * g:G * g + n, :]
                else:
                    if g == 0:
                        dve.wait_ge(h_ready[1], 2 * j)
                    in0 = h[1][:, None, :].to_broadcast([128, n, N])
                    in1 = xwide[:, par, G * g:G * g + n, :]
                number = before(kind, j, pos)
                if kind == "W":
                    ready(dve, whole_used, number - WHOLE_RING + 1)
                    dst = z_whole[0:rows, slot("W", pair, par, pos, WHOLE_RING), 0:n, :]
                elif kind == "P":
                    ready(dve, lo_made["P"], number - RAW_RING + 1)
                    dst = z_raw[0:rows, slot("P", pair, par, pos, RAW_RING), 0:n, :]
                else:
                    ready(dve, lo_made["V"], number)
                    dst = z_psum[0:rows, 0:n, :]
                nc.vector.tensor_tensor(dst, in0, in1, ALU.mult).then_inc(made[kind], 1)

            def subtract(pair, par, pos):
                j = step_of(pair, par)
                layer, g, _ = order(j)[pos]
                number = before("PV", j, pos)
                dve.wait_ge(hi_made, number + 1)
                ready(dve, split_used, number - LO_RING + 1)
                take(nc.vector, z_psum,
                     z_hi[:, slot("PV", pair, par, pos, HI_RING)],
                     z_lo[:, slot("PV", pair, par, pos, LO_RING)], layer, g).then_inc(lo_made["V"], 1)

            def sum_direct(j, half):
                dve.wait_ge(acc_read[1], j + 1)
                nc.vector.tensor_reduce(sums01[:, bass.ds(BB * j, BB)],
                                        direct[:, half, :].rearrange("p (b d) -> p b d", d=DIM),
                                        AX_X, ALU.add).then_inc(summed, 1)

            def sum_last(j):
                dve.wait_ge(acc_read[2], j + 1)
                nc.vector.tensor_reduce(sums2[:, bass.ds(BB * j, BB)],
                                        last[:].rearrange("p (b d) -> p b d", d=DIM),
                                        AX_X, ALU.add).then_inc(summed, 1)

            def step(pair, par):
                j = step_of(pair, par)
                late = []
                if (not isinstance(j, int) or j > 0) and order(j - 1)[-1][2] == "V":
                    late.append((V_LAG - 1, pair + par - 1, 1 - par, len(order(j - 1)) - 1))
                for pos, (layer, g, kind) in enumerate(order(j)):
                    while late and (kind == "V" or pos > late[0][0]):
                        subtract(*late.pop(0)[1:])
                    if pos == SUM1_AT and not (isinstance(j, int) and j < 1):
                        sum_direct(j - 1, par)
                    if pos == SUM2_AT and not (isinstance(j, int) and j < 2):
                        sum_last(j - 2)
                    products(pair, par, pos)
                    if kind == "V":
                        late.append((pos + V_LAG, pair, par, pos))
                for p in late[:-1] if order(j)[-1][2] == "V" else late:
                    subtract(*p[1:])

            dve.wait_ge(w0_in, 32)
            nc.vector.tensor_tensor(w0[:], w0[:], w0t, ALU.add).then_inc(w0_folded, 1)
            for pos in range(len(order(-1))):
                products(-1, 0, pos)
            a, n = SPLIT_FROM[1], SPLIT_COUNT[1]
            dve.wait_ge(w_hi_made, len(SPLIT0) + 1)
            nc.vector.tensor_tensor(w_lo[:, a:a + n, :], stage[1][:, 0:n, :], w_hi[:, a:a + n, :].bitcast(F32),
                                    ALU.subtract).then_inc(w1_lo_made, 1)
            step(-1, 1)
            for par in range(2):
                step(0, par)
            with dve.Fori(1, PAIRS - 1) as pair:
                for par in range(2):
                    step(pair, par)
            for par in range(2):
                step(PAIRS - 1, par)
            subtract(PAIRS - 1, 1, len(order(BLOCKS)) - 1)
            sum_last(BLOCKS - 1)

        @block.gpsimd
        def _(pool):
            def subtract(pair, par, pos):
                j = step_of(pair, par)
                layer, g, _ = order(j)[pos]
                number = before("PV", j, pos)
                pool.wait_ge(hi_made, number + 1)
                ready(pool, split_used, number - LO_RING + 1)
                take(nc.gpsimd, z_raw[:, slot("P", pair, par, pos, RAW_RING)],
                     z_hi[:, slot("PV", pair, par, pos, HI_RING)],
                     z_lo[:, slot("PV", pair, par, pos, LO_RING)], layer, g).then_inc(lo_made["P"], 1)

            def step(pair, par):
                j = step_of(pair, par)
                for pos, (layer, g, kind) in enumerate(order(j)):
                    if (layer, g) == SPLIT2_BEFORE and isinstance(j, int) and j == 0:
                        split(stage[2][:, 0:SPLIT_COUNT[2], :], SPLIT_FROM[2], SPLIT_COUNT[2], 128, len(SPLIT0) + 2)
                    if kind == "P":
                        subtract(pair, par, pos)

            def split(raw, a, n, rows, hi_count):
                pool.wait_ge(w_hi_made, hi_count)
                nc.gpsimd.tensor_tensor(w_lo[0:rows, a:a + n, :], raw, w_hi[0:rows, a:a + n, :].bitcast(F32),
                                        ALU.subtract).then_inc(w_lo_made, 1)

            for i, (a, ts) in enumerate(SPLIT0):
                split(w0[:, ts[0]:ts[-1] + 1, :], a, len(ts), P0, i + 1)
            for par in range(2):
                step(-1, par)
            with pool.Fori(0, PAIRS - 1) as pair:
                for par in range(2):
                    step(pair, par)
            for par in range(2):
                step(PAIRS - 1, par)

        @block.tensor
        def _(pe):
            def contract(pair, par, pos):
                j = step_of(pair, par)
                layer, g, kind = order(j)[pos]
                ts = tiles_of(layer, g)
                last_g = g == len(KINDS[layer]) - 1
                dst = acc[layer][:, :]
                number = before(kind, j, pos)

                def matmul(w, z, t, first, final):
                    rows = rows_of(layer, t)
                    return nc.tensor.matmul(dst, w[0:rows, PLACE[layer, t], :], z[0:rows, t - G * g, :],
                                            start=first and t == 0,
                                            stop=final and t == TILES[layer] - 1)

                if g == 0:
                    if layer == 2 and isinstance(j, int) and j == 1:
                        pe.wait_ge(w_lo_made, len(SPLIT0) + 1)
                    ready(pe, acc_read[layer], j + (1, 0, -1)[layer])
                if kind == "W":
                    pe.wait_ge(made["W"], number + 1)
                    z = z_whole[:, slot("W", pair, par, pos, WHOLE_RING)]
                    for t in ts:
                        mm = matmul(w0 if layer == 0 else w_whole, z, t, True, True)
                    mm.then_inc(whole_used, 1)
                    return
                if isinstance(j, int) and j == -1:
                    pe.wait_ge(w_lo_made, len(SPLIT0))
                pe.wait_ge(hi_made, before("PV", j, pos) + 1)
                hi = z_hi[:, slot("PV", pair, par, pos, HI_RING)]
                stacked = ts[-1] if layer and last_g else None
                ts = [t for t in ts if t != stacked]
                for t in ts:
                    matmul(w_hi, hi, t, True, False)
                for t in ts:
                    matmul(w_lo, hi, t, False, False)
                pe.wait_ge(lo_made[kind], number + 1)
                lo = z_lo[:, slot("PV", pair, par, pos, LO_RING)]
                for t in ts:
                    mm = matmul(w_hi, lo, t, False, stacked is None)
                if stacked is not None:
                    matmul(w_hi, hi, stacked, False, False)
                    mm = matmul(w_lo, hi, stacked, False, True)
                mm.then_inc(split_used, 1)

            def step(pair, par):
                for pos in range(len(order(step_of(pair, par)))):
                    contract(pair, par, pos)

            pe.wait_ge(w0_folded, 1)
            step(-1, 0)
            pe.wait_ge(w_whole_in, 16)
            pe.wait_ge(w1_lo_made, 1)
            step(-1, 1)
            for par in range(2):
                step(0, par)
            with pe.Fori(1, PAIRS - 1) as pair:
                for par in range(2):
                    step(pair, par)
            for par in range(2):
                step(PAIRS - 1, par)

        @block.scalar
        def _(act):
            def high_part(pair, par, pos):
                j = step_of(pair, par)
                layer, g, kind = order(j)[pos]
                n = len(tiles_of(layer, g))
                rows = P0 if layer == 0 else 128
                act.wait_ge(made[kind], before(kind, j, pos) + 1)
                ready(act, split_used, before("PV", j, pos) - HI_RING + 1)
                if kind == "P":
                    src = z_raw[0:rows, slot("P", pair, par, pos, RAW_RING), 0:n, :]
                else:
                    src = z_psum[0:rows, 0:n, :]
                nc.scalar.copy(z_hi[0:rows, slot("PV", pair, par, pos, HI_RING), 0:n, :], src).then_inc(hi_made, 1)

            def relu(dst, src, layer, rows):
                return nc.scalar.activation(dst, src, ACT.Relu, bias=bias[rows, layer:layer + 1])

            def wait_acc(layer, j):
                if KINDS[layer][-1] == "W":
                    act.wait_ge(whole_used, before("W", j, place_of(j, layer)) + 1)
                else:
                    act.wait_ge(split_used, before("PV", j, place_of(j, layer)) + 1)

            def copy_xrep(j):
                act.wait_ge(xrep_in, 16 * PER * (j + 2))
                if not isinstance(j, int) or j >= 0:
                    act.wait_ge(*made_all(j - 1, 0))
                nc.scalar.copy(xrep_psum[0:P0, :], xrep[:, :]).then_inc(xrep_ready, 1)

            def relu0(j, half):
                wait_acc(0, j)
                if not isinstance(j, int) or j >= 0:
                    act.wait_ge(*made_all(j, 1))
                a = acc[0]
                relu(h[0][0:HALF, :], a[0:HALF, :], 0, slice(0, HALF)).then_inc(h_ready[0], 1)
                relu(h[0][HALF:, :], a[0:HALF, :], 0, slice(0, HALF)).then_inc(h_ready[0], 1)
                relu(direct[HALF:, half, :], a[HALF:, :], 0, slice(HALF, SIZE)).then_inc(acc_read[0], 1)

            def relu1(j, half):
                wait_acc(1, j - 1)
                if not isinstance(j, int) or j > 1:
                    act.wait_ge(*made_all(j - 1, 2))
                a = acc[1]
                relu(h[1][0:HALF, :], a[HALF:, :], 1, slice(HALF, SIZE)).then_inc(h_ready[1], 1)
                relu(h[1][HALF:, :], a[HALF:, :], 1, slice(HALF, SIZE)).then_inc(h_ready[1], 1)
                relu(direct[0:HALF, half, :], a[0:HALF, :], 1, slice(0, HALF)).then_inc(acc_read[1], 1)

            def relu2(j):
                wait_acc(2, j - 1)
                relu(last[:], acc[2][:, :], 2, slice(0, SIZE)).then_inc(acc_read[2], 1)

            def step(pair, par):
                j = step_of(pair, par)

                def has(low, high):
                    return not isinstance(j, int) or low <= j <= high

                for pos, (layer, g, kind) in enumerate(order(j)):
                    if (layer, g) == (0, 0) if isinstance(j, int) and j == 0 else \
                            pos == XREP_AT and has(0, BLOCKS - 2):
                        copy_xrep(j)
                    if pos == RELU0_AT and has(1, BLOCKS - 2):
                        relu0(j, par)
                    if pos == RELU1_AT and has(1, BLOCKS):
                        relu1(j, par)
                    if pos == RELU2_AT and has(2, BLOCKS):
                        relu2(j)
                    if isinstance(j, int) and j == 0 and (layer, g) == SPLIT2_BEFORE:
                        split_layer(2)
                    if kind != "W":
                        high_part(pair, par, pos)
                if isinstance(j, int) and j == 0:
                    relu0(j, par)

            def split(raw, a, n, rows):
                nc.scalar.copy(w_hi[0:rows, a:a + n, :], raw).then_inc(w_hi_made, 1)

            def split_layer(layer):
                act.wait_ge(w_staged[layer], 16)
                split(stage[layer][:, 0:SPLIT_COUNT[layer], :], SPLIT_FROM[layer], SPLIT_COUNT[layer], 128)

            copy_xrep(-1)
            act.wait_ge(w0_folded, 1)
            for a, ts in SPLIT0:
                split(w0[:, ts[0]:ts[-1] + 1, :], a, len(ts), P0)
            for pos, (_, _, kind) in enumerate(order(-1)):
                if kind != "W":
                    high_part(-1, 0, pos)
            split_layer(1)
            act.wait_ge(bias_in, 16)
            relu0(-1, 0)
            step(-1, 1)
            for par in range(2):
                step(0, par)
            with act.Fori(1, PAIRS - 1) as pair:
                for par in range(2):
                    step(pair, par)
            for par in range(2):
                step(PAIRS - 1, par)
            relu2(BLOCKS + 1)


def kernel(r_x, L0_rec_W0, L0_rec_W1, L0_rec_W2, L0_rec_b0, L0_rec_b1, L0_rec_b2):
    import numpy as np
    import concourse.bacc as bacc
    from concourse.bass_utils import run_bass_kernel_spmd

    x = np.asarray(r_x).transpose(1, 0, 2).reshape(FIELDS, COLS)
    w0 = np.asarray(L0_rec_W0).reshape(FIELDS, FIELDS, SIZE)
    w0a = np.zeros((PER, FIELDS, T0, SIZE), np.float32)
    w0b = np.zeros((PER, FIELDS, T0, SIZE), np.float32)
    f = np.arange(FIELDS)
    for s in range(SHIFTS):
        g = (f + s) % FIELDS
        w0a[s % PER, :, s // PER] = w0[f, g]
        if s:
            w0b[s % PER, :, s // PER] = w0[g, f]

    def tiled(w):
        w = np.concatenate([w, w[-HALF:]])
        return w.reshape(T12, 128, SIZE).transpose(1, 0, 2)

    def some(w, layer, whole):
        return w[:, [t for g, k in enumerate(KINDS[layer]) if (k == "W") == whole for t in tiles_of(layer, g)]]

    def swapped(w):
        return np.concatenate([w[..., HALF:], w[..., :HALF]], axis=-1)

    w1 = tiled(swapped(np.asarray(L0_rec_W1)))
    w2 = tiled(np.asarray(L0_rec_W2))
    arrays = {
        "x2": np.concatenate([x, x]),
        "w0a": w0a.reshape(P0, T0, SIZE),
        "w0b": w0b.reshape(P0, T0, SIZE),
        "w1": some(w1, 1, False),
        "w2": some(w2, 2, False),
        "w_rest": np.concatenate([some(w1, 1, True), some(w2, 2, True)], axis=1),
        "b": np.stack([np.asarray(L0_rec_b0), swapped(np.asarray(L0_rec_b1)), np.asarray(L0_rec_b2)], axis=1),
    }
    arrays = {k: np.ascontiguousarray(v) for k, v in arrays.items()}
    nc = bacc.Bacc("TRN2", target_bir_lowering=False, num_devices=1,
                   dynamic_dma_scratch_size=1024)
    args = [nc.dram_tensor(k, v.shape, F32, kind="ExternalInput").ap() for k, v in arrays.items()]
    out = nc.dram_tensor("out", (2 * SIZE, BATCH), F32, kind="ExternalOutput").ap()
    cin(nc, *args, out)
    r = run_bass_kernel_spmd(nc, [arrays], core_ids=[0])
    return np.ascontiguousarray(r.results[0]["out"].T)
```
